# Optimizing a Trainium2 kernel written in Bass

```python
import numpy as np
import jax
import jax.numpy as jnp

def _softmax(x, axis=-1):
    return jax.nn.softmax(x, axis=axis)

def _gelu(x):
    return jax.nn.gelu(x, approximate=True)

def _silu(x):
    return jax.nn.silu(x)

def _sigmoid(x):
    return jax.nn.sigmoid(x)

def _layernorm(x, axis=-1, eps=1e-05):
    m = jnp.mean(x, axis=axis, keepdims=True)
    v = jnp.var(x, axis=axis, keepdims=True)
    return (x - m) / jnp.sqrt(v + eps)

def _scatter_add(tgt, idx, src, axis=0):
    return tgt.at[idx].add(src)

def _segment_sum(src, seg, n):
    return jax.ops.segment_sum(src, seg, n)
kernel_name = 'mk_cond_resid_d2_seqx_r2_b19722'

def setup_inputs(seed: int=0):
    np.random.seed(seed)
    _w = jnp.asarray

    def _rec_inputs():
        import jax
        import jax.numpy as jnp
        _rk = jax.random.key(seed)
        x = -0.000125 + 0.9999 * jax.random.normal(jax.random.fold_in(_rk, 1), (8, 512, 2048), jnp.float32)
        _lenS = 512 - jax.random.randint(jax.random.fold_in(_rk, 7), (8,), 0, max(1, 512 // 4) + 1, jnp.int32)
        _lenS2 = 512 - jax.random.randint(jax.random.fold_in(_rk, 8), (8,), 0, max(1, 512 // 4) + 1, jnp.int32)
        itok_B_3_7 = jax.random.randint(jax.random.fold_in(_rk, 11), (8,), 3, 8, jnp.int32)
        itok_B_0_23 = jax.random.randint(jax.random.fold_in(_rk, 12), (8,), 0, 24, jnp.int32)
        return (x, itok_B_3_7, itok_B_0_23)
    x, itok_B_3_7, itok_B_0_23 = _rec_inputs()

    def _L0_cond_setup():
        import jax, jax.numpy as jnp
        import numpy as np
        MAX_LORAS, OUT, IN = (8, 2048, 2048)
        B, S = (4, 1024)
        key = jax.random.key(seed)
        k1, k2, k3 = jax.random.split(key, 3)
        x = jax.random.normal(k1, (B, S, IN), dtype=jnp.float32)
        weight = jax.random.normal(k2, (MAX_LORAS, OUT, IN), dtype=jnp.float32) * 0.02
        adapter_ids = jax.random.randint(k3, (B,), 0, MAX_LORAS, dtype=jnp.int32)
        return {'x': x, 'weight': weight, 'adapter_ids': adapter_ids}
    _L0_cond_all = _L0_cond_setup()
    _L0_cond_in = {k: v for k, v in _L0_cond_all.items() if k in ('weight',)}
    del _L0_cond_all

    def _L1_cond_setup():
        import jax, jax.numpy as jnp
        import numpy as np
        R = 16
        ALPHA = 32
        SCALING = ALPHA / R
        SLOTS = 32
        IN_F = 2048
        OUT_F = 2048
        B, T = (8, 512)
        key = jax.random.key(seed)
        k1, k2, k3, k4, k5, k6 = jax.random.split(key, 6)
        x = jax.random.normal(k1, (B, T, IN_F), dtype=jnp.float32)
        adapter_mapping = jax.random.randint(k2, (B,), 0, SLOTS, dtype=jnp.int32)
        W = jax.random.normal(k3, (OUT_F, IN_F), dtype=jnp.float32) * 0.02
        b = jax.random.normal(k4, (OUT_F,), dtype=jnp.float32) * 0.02
        lora_As = jax.random.normal(k5, (SLOTS, IN_F, R), dtype=jnp.float32) * 0.02
        lora_Bs = jax.random.normal(k6, (SLOTS, R, OUT_F), dtype=jnp.float32) * 0.02
        return {'x': x, 'adapter_mapping': adapter_mapping, 'W': W, 'b': b, 'lora_As': lora_As, 'lora_Bs': lora_Bs}
    _L1_cond_all = _L1_cond_setup()
    _L1_cond_in = {k: v for k, v in _L1_cond_all.items() if k in ('W', 'b', 'lora_As', 'lora_Bs')}
    del _L1_cond_all
    return {'x': x, 'itok_B_3_7': itok_B_3_7, 'itok_B_0_23': itok_B_0_23, 'L0_cond_weight': _L0_cond_in['weight'], 'L1_cond_W': _L1_cond_in['W'], 'L1_cond_b': _L1_cond_in['b'], 'L1_cond_lora_As': _L1_cond_in['lora_As'], 'L1_cond_lora_Bs': _L1_cond_in['lora_Bs']}

def reference(x, itok_B_3_7, itok_B_0_23, L0_cond_weight, L1_cond_W, L1_cond_b, L1_cond_lora_As, L1_cond_lora_Bs):
    import jax
    import jax.numpy as jnp

    def _L0_cond_ref(x, weight, adapter_ids):
        import jax, jax.numpy as jnp
        import numpy as np
        MAX_LORAS, OUT, IN = (8, 2048, 2048)
        B, S = (4, 1024)
        w = weight[adapter_ids]
        return jnp.einsum('bsi,boi->bso', x, w)

    def _L1_cond_ref(x, adapter_mapping, W, b, lora_As, lora_Bs):
        import jax, jax.numpy as jnp
        import numpy as np
        R = 16
        ALPHA = 32
        SCALING = ALPHA / R
        SLOTS = 32
        IN_F = 2048
        OUT_F = 2048
        B, T = (8, 512)
        base_out = jnp.einsum('bti,oi->bto', x, W) + b
        A = lora_As[adapter_mapping]
        Bm = lora_Bs[adapter_mapping]
        lora_h = jnp.einsum('bti,bir->btr', x, A)
        lora_out = jnp.einsum('btr,bro->bto', lora_h, Bm)
        return base_out + lora_out * SCALING
    x = x + _L0_cond_ref(x, L0_cond_weight, itok_B_3_7)
    x = x + _L1_cond_ref(x, itok_B_0_23, L1_cond_W, L1_cond_b, L1_cond_lora_As, L1_cond_lora_Bs)
    return x

_drawn_inputs = setup_inputs


def setup_inputs(seed=0):
    import zlib

    import numpy as np

    out = dict(_drawn_inputs(seed))
    spreads = {}
    factors = {'L1_cond_b': 5.385}
    for name, (base, spread) in spreads.items():
        noise = np.random.default_rng([zlib.crc32(name.encode()), seed]).standard_normal(out[name].shape)
        drawn = base * np.exp(spread * noise) if base else spread * noise
        out[name] = jnp.asarray(drawn.astype(out[name].dtype))
    for name, factor in factors.items():
        out[name] = (out[name] * factor).astype(out[name].dtype)
    return out
```

```python
from contextlib import ExitStack

import concourse.bass as bass
from concourse import mybir

P = 128
F32 = mybir.dt.float32
F32R = mybir.dt.float32r
I32 = mybir.dt.int32
ALU = mybir.AluOpType
ACT = mybir.ActivationFunctionType

LORA_SCALING = 32.0 / 16.0


def build(nc, xT, ids0, ids1, w0T, w1T, bias, lora_a, lora_b, yT):
    NB, XCHUNKS, _, KX, TOK = xT.shape
    ADAPTERS, NT, _, KT, _ = w0T.shape
    SLOTS, _, _, R = lora_a.shape
    D = KT * P
    RAW = 2
    TILES = 2 * NT
    GROUP = 2 * R
    assert GROUP == 32 and NT % 2 == 0 and XCHUNKS == NT // 2 and KX * XCHUNKS == KT

    with ExitStack() as ctx:
        def sb(name, shape, dt=F32):
            return ctx.enter_context(nc.sbuf_tensor(name, shape, dt))

        def psum(name, shape):
            return ctx.enter_context(nc.psum_tensor(name, shape, F32))

        def sem(name):
            return ctx.enter_context(nc.semaphore(name))

        x_hi = sb("x_hi", [P, KT, TOK], F32R)
        x_lo = sb("x_lo", [P, KT, TOK], F32R)
        x1_hi = sb("x1_hi", [P, KT, TOK], F32R)
        x1_lo = sb("x1_lo", [P, KT, TOK], F32R)
        w_raw = [sb(f"w_raw{s}", [P, KT, P]) for s in range(RAW)]
        w_hi = [sb(f"w_hi{s}", [P, KT, P], F32R) for s in range(RAW)]
        w_lo = [sb(f"w_lo{s}", [P, KT, P], F32R) for s in range(RAW)]
        a_raw = sb("a_raw", [P, KT, R])
        a_mix = sb("a_mix", [P, KT, P // GROUP, GROUP], F32R)
        b_raw = sb("b_raw", [P, D])
        b_mix = [sb(f"b_mix{s}", [P, P], F32R) for s in range(RAW)]
        h_mix = sb("h_mix", [P, TOK], F32R)
        bias_sb = sb("bias_sb", [P, NT])
        ids_sb = sb("ids_sb", [1, 2, NB], I32)
        out_slots = sb("out_slots", [P, RAW, TOK])
        x1_raw = y_out = out_slots[:]
        x_raw = sb("x_raw", [P, KX, TOK])[:]

        sums = [psum(f"sums{s}", [P, TOK]) for s in range(RAW)]
        h_sum = psum("h_sum", [P, TOK])

        ids_loaded = sem("ids_loaded")
        bias_loaded = sem("bias_loaded")
        w_loaded = [sem(f"w_loaded{s}") for s in range(RAW)]
        w_raw_free = sem("w_raw_free")
        w_hi_done = sem("w_hi_done")
        w_ready = sem("w_ready")
        x_loaded = sem("x_loaded")
        x_hi_done = sem("x_hi_done")
        x_ready = sem("x_ready")
        ab_loaded = sem("ab_loaded")
        a_hi_done = sem("a_hi_done")
        a_ready = sem("a_ready")
        b_hi_done = sem("b_hi_done")
        b_ready = sem("b_ready")
        tile_done = sem("tile_done")
        sums_free = sem("sums_free")
        x1_part = sem("x1_part")
        x1_sum = sem("x1_sum")
        x1_hi_done = sem("x1_hi_done")
        x1_ready = sem("x1_ready")
        h_done = sem("h_done")
        h_hi_done = sem("h_hi_done")
        h_ready = sem("h_ready")
        y_part = sem("y_part")
        y_ready = sem("y_ready")
        y_stored = sem("y_stored")
        y_slot_free = sem("y_slot_free")

        block = ctx.enter_context(nc.Block())

        @block.sync
        def _(sp):
            sp.dma_start(ids_sb[:, 0, :], ids0).then_inc(ids_loaded, 16)
            sp.dma_start(ids_sb[:, 1, :], ids1).then_inc(ids_loaded, 16)
            sp.dma_start(bias_sb[:], bias).then_inc(bias_loaded, 16)
            sp.wait_ge(ids_loaded, 32)
            with sp.Fori(0, NB) as b:
                adapter = sp.value_load(ids_sb[0:1, 0, bass.ds(b, 1)], min_val=0, max_val=ADAPTERS - 1)
                with sp.Fori(0, NT // 2) as pair:
                    for s in range(RAW):
                        sp.wait_ge(w_raw_free, b * TILES + pair * 2 + s + 1)
                        sp.dma_start(w_raw[s][:], w0T[bass.ds(adapter, 1), bass.ds(pair * 2 + s, 1)]
                                     .rearrange("a t p k o -> (a t p) k o")).then_inc(w_loaded[s], 16)
                with sp.Fori(0, NT // 2) as pair:
                    for s in range(RAW):
                        sp.wait_ge(w_raw_free, b * TILES + NT + pair * 2 + s + 1)
                        sp.dma_start(w_raw[s][:], w1T[bass.ds(pair * 2 + s, 1)]
                                     .rearrange("t p k o -> (t p) k o")).then_inc(w_loaded[s], 16)

        @block.gpsimd
        def _(pool):
            pool.sem_inc(y_slot_free, RAW)

            def load_x(b, chunk):
                pool.dma_start(x_raw, xT[bass.ds(b, 1), bass.ds(chunk, 1)]
                               .rearrange("b c p k n -> (b c p) k n")).then_inc(x_loaded, 16)

            load_x(0, 0)
            with pool.Fori(1, XCHUNKS) as chunk:
                pool.wait_ge(x_ready, chunk)
                load_x(0, chunk)
            pool.wait_ge(ids_loaded, 32)
            with pool.Fori(0, NB) as b:
                slot = pool.value_load(ids_sb[0:1, 1, bass.ds(b, 1)], min_val=0, max_val=SLOTS - 1)
                pool.dma_start(a_raw[:], lora_a[bass.ds(slot, 1)]
                               .rearrange("s p k r -> (s p) k r")).then_inc(ab_loaded, 16)
                for copy in range(P // R):
                    pool.dma_start(b_raw[copy * R:(copy + 1) * R, :], lora_b[bass.ds(slot, 1)]
                                   .rearrange("s r n -> (s r) n")).then_inc(ab_loaded, 16)
                with pool.Fori(0, NT // 2) as pair:
                    with pool.If(b < NB - 1):
                        pool.wait_ge(x_ready, (b + 1) * XCHUNKS + pair)
                        following = nc.s_assert_within(
                            b + 1, 1, NB - 1, skip_runtime_bounds_check_because="only where b < NB - 1")
                        load_x(following, pair)
                    for s in range(RAW):
                        pool.wait_ge(y_ready, b * NT + pair * 2 + s + 1)
                        pool.dma_start(yT[bass.ds(b, 1), bass.ds(pair * 2 + s, 1)]
                                       .rearrange("b t p n -> (b t p) n"), y_out[:, s, :]
                                       ).then_inc(y_stored, 16)
                        pool.wait_ge(y_stored, (b * NT + pair * 2 + s + 1) * 16)
                        pool.sem_inc(y_slot_free, 1)

        @block.scalar
        def _(act):
            def w_hi_part(s, n):
                act.wait_ge(w_loaded[s], n * 8 + (16 - 8 * s))
                act.activation(w_hi[s][:], w_raw[s][:], ACT.Copy).then_inc(w_hi_done, 1)

            def x_hi_part(b, chunk):
                act.wait_ge(x_loaded, (b * XCHUNKS + chunk + 1) * 16)
                act.activation(x_hi[:, bass.ds(chunk * KX, KX), :], x_raw, ACT.Copy).then_inc(x_hi_done, 1)

            w_hi_part(0, 0)
            with act.Fori(0, XCHUNKS) as chunk:
                x_hi_part(0, chunk)
            w_hi_part(1, 1)
            with act.Fori(0, NB) as b:
                act.wait_ge(ab_loaded, (b + 1) * (16 * (1 + P // R)))
                for q in range(P // GROUP):
                    act.activation(a_mix[:, :, q, 0:R], a_raw[:], ACT.Copy).then_inc(a_hi_done, 1)
                with act.Fori(0, NT // 2) as pair:
                    for s in range(RAW):
                        n = b * TILES + pair * 2 + s
                        act.wait_ge(tile_done, n + 1)
                        w_hi_part(s, n + RAW)
                        act.wait_ge(x1_sum, b * NT + pair * 2 + s + 1)
                        act.activation(x1_hi[:, bass.ds(pair * 2 + s, 1), :], x1_raw[:, s:s + 1, :],
                                       ACT.Copy).then_inc(x1_hi_done, 1)
                act.wait_ge(h_done, b + 1)
                act.activation(h_mix[:], h_sum[:], ACT.Copy).then_inc(h_hi_done, 1)
                with act.Fori(0, NT // 2) as pair:
                    for s in range(RAW):
                        t = pair * 2 + s
                        n = b * TILES + NT + t
                        act.activation(b_mix[s][:], b_raw[:, bass.ds(t * P, P)], ACT.Copy,
                                       scale=LORA_SCALING).then_inc(b_hi_done, 1)
                        with act.If(n < NB * TILES - RAW):
                            act.wait_ge(tile_done, n + 1)
                            w_hi_part(s, n + RAW)
                    with act.If(b < NB - 1):
                        act.wait_ge(x1_ready, (b + 1) * NT)
                        x_hi_part(b + 1, pair)

        @block.vector
        def _(dve):
            dve.sem_inc(w_raw_free, RAW)
            dve.sem_inc(sums_free, RAW)

            def w_lo_part(s, n):
                dve.wait_ge(w_hi_done, n + 1)
                dve.tensor_tensor(w_lo[s][:], w_raw[s][:], w_hi[s][:].bitcast(F32),
                                  ALU.subtract).then_inc(w_ready, 1)
                dve.wait_ge(w_ready, n + 1)
                dve.sem_inc(w_raw_free, 1)

            def x_lo_part(b, chunk):
                dve.wait_ge(x_hi_done, b * XCHUNKS + chunk + 1)
                dve.tensor_tensor(x_lo[:, bass.ds(chunk * KX, KX), :], x_raw,
                                  x_hi[:, bass.ds(chunk * KX, KX), :].bitcast(F32),
                                  ALU.subtract).then_inc(x_ready, 1)

            w_lo_part(0, 0)
            with dve.Fori(0, XCHUNKS) as chunk:
                x_lo_part(0, chunk)
            w_lo_part(1, 1)
            dve.wait_ge(bias_loaded, 16)
            with dve.Fori(0, NB) as b:
                dve.wait_ge(a_hi_done, (b + 1) * (P // GROUP))
                for q in range(P // GROUP):
                    dve.tensor_tensor(a_mix[:, :, q, R:GROUP], a_raw[:], a_mix[:, :, q, 0:R].bitcast(F32),
                                      ALU.subtract).then_inc(a_ready, 1)
                with dve.Fori(0, NT // 2) as pair:
                    for s in range(RAW):
                        t = pair * 2 + s
                        n = b * TILES + t
                        dve.wait_ge(tile_done, n + 1)
                        dve.tensor_tensor(x1_raw[:, s:s + 1, :], sums[s][:].unsqueeze(1),
                                          x_lo[:, bass.ds(t, 1), :].bitcast(F32),
                                          ALU.add).then_inc(x1_part, 1)
                        dve.wait_ge(x1_part, b * NT + t + 1)
                        dve.sem_inc(sums_free, 1)
                        dve.tensor_tensor(x1_raw[:, s:s + 1, :], x1_raw[:, s:s + 1, :],
                                          x_hi[:, bass.ds(t, 1), :].bitcast(F32),
                                          ALU.add).then_inc(x1_sum, 1)
                        dve.wait_ge(x1_hi_done, b * NT + t + 1)
                        dve.tensor_tensor(x1_lo[:, bass.ds(t, 1), :], x1_raw[:, s:s + 1, :],
                                          x1_hi[:, bass.ds(t, 1), :].bitcast(F32),
                                          ALU.subtract).then_inc(x1_ready, 1)
                        w_lo_part(s, n + RAW)
                dve.wait_ge(h_hi_done, b + 1)
                for q in range(1, P // GROUP, 2):
                    rows = slice(q * GROUP, (q + 1) * GROUP)
                    dve.tensor_tensor(h_mix[rows, :], h_sum[rows, :], h_mix[rows, :].bitcast(F32),
                                      ALU.subtract).then_inc(h_ready, 1)
                with dve.Fori(0, NT // 2) as pair:
                    for s in range(RAW):
                        t = pair * 2 + s
                        n = b * TILES + NT + t
                        dve.wait_ge(b_hi_done, b * NT + t + 1)
                        dve.scalar_tensor_tensor(out=b_mix[s][P // 2:P, :],
                                                 in0=b_raw[P // 2:P, bass.ds(t * P, P)], scalar=LORA_SCALING,
                                                 in1=b_mix[s][P // 2:P, :].bitcast(F32), op0=ALU.mult,
                                                 op1=ALU.subtract).then_inc(b_ready, 1)
                        dve.wait_ge(tile_done, n + 1)
                        dve.wait_ge(y_slot_free, b * NT + t + 1)
                        dve.scalar_tensor_tensor(out=y_out[:, s, :], in0=sums[s][:],
                                                 scalar=bias_sb[:, bass.ds(t, 1)],
                                                 in1=x1_lo[:, bass.ds(t, 1), :].squeeze(1).bitcast(F32),
                                                 op0=ALU.add, op1=ALU.add).then_inc(y_part, 1)
                        dve.wait_ge(y_part, b * NT + t + 1)
                        dve.sem_inc(sums_free, 1)
                        dve.tensor_tensor(y_out[:, s:s + 1, :], y_out[:, s:s + 1, :],
                                          x1_hi[:, bass.ds(t, 1), :].bitcast(F32),
                                          ALU.add).then_inc(y_ready, 1)
                        with dve.If(n < NB * TILES - RAW):
                            w_lo_part(s, n + RAW)
                    with dve.If(b < NB - 1):
                        x_lo_part(b + 1, pair)

        @block.tensor
        def _(pe):
            def tile(s, n, hi, lo, wait_k, last):
                pe.wait_ge(w_ready, n + 1)
                pe.wait_ge(sums_free, n + 1)
                for k in range(KT):
                    wait_k(k)
                    pe.matmul(sums[s][:], w_hi[s][:, k, :], hi[:, k, :], start=(k == 0), stop=False)
                    pe.matmul(sums[s][:], w_hi[s][:, k, :], lo[:, k, :], start=False, stop=False)
                    mm = pe.matmul(sums[s][:], w_lo[s][:, k, :], hi[:, k, :], start=False,
                                   stop=last and k == KT - 1)
                return mm

            with pe.Fori(0, NB) as b:
                with pe.Fori(0, NT // 2) as pair:
                    for s in range(RAW):
                        def x_chunk_ready(k, s=s):
                            if s == 0 and k % KX == 0:
                                pe.wait_ge(x_ready, b * XCHUNKS + k // KX + 1)
                        tile(s, b * TILES + pair * 2 + s, x_hi, x_lo, x_chunk_ready, True).then_inc(tile_done, 1)
                pe.wait_ge(a_ready, (b + 1) * (P // GROUP))
                pe.wait_ge(x1_ready, b * NT + NT - 1)
                for k in range(KT):
                    if k == KT - 1:
                        pe.wait_ge(x1_ready, b * NT + NT)
                    a_k = a_mix[:, k, :, :].rearrange("p q r -> p (q r)")
                    pe.matmul(h_sum[:], a_k, x1_hi[:, k, :], start=(k == 0), stop=False)
                    mm = pe.matmul(h_sum[:], a_k, x1_lo[:, k, :], start=False, stop=(k == KT - 1))
                mm.then_inc(h_done, 1)
                with pe.Fori(0, NT // 2) as pair:
                    for s in range(RAW):
                        t = pair * 2 + s
                        tile(s, b * TILES + NT + t, x1_hi, x1_lo, lambda k: None, False)
                        pe.wait_ge(h_ready, (b + 1) * 2)
                        pe.wait_ge(b_ready, b * NT + t + 1)
                        pe.matmul(sums[s][:], b_mix[s][:], h_mix[:], start=False,
                                  stop=True).then_inc(tile_done, 1)


def kernel(x, itok_B_3_7, itok_B_0_23, L0_cond_weight, L1_cond_W, L1_cond_b, L1_cond_lora_As, L1_cond_lora_Bs):
    import numpy as np
    import concourse.bacc as bacc
    from concourse.bass_utils import run_bass_kernel_spmd

    nb, tok, d = x.shape
    nt, kt, kx = d // P, d // P, 2
    c = np.ascontiguousarray
    arrays = {
        "xT": c(x.reshape(nb, tok, kt // kx, kx, P).transpose(0, 2, 4, 3, 1)),
        "ids0": c(itok_B_3_7.reshape(1, nb)),
        "ids1": c(itok_B_0_23.reshape(1, nb)),
        "w0T": c(L0_cond_weight.reshape(-1, nt, P, kt, P).transpose(0, 1, 4, 3, 2)),
        "w1T": c(L1_cond_W.reshape(nt, P, kt, P).transpose(0, 3, 2, 1)),
        "bias": c(L1_cond_b.reshape(nt, P).T),
        "lora_a": c(L1_cond_lora_As.reshape(-1, kt, P, L1_cond_lora_As.shape[2]).transpose(0, 2, 1, 3)),
        "lora_b": c(L1_cond_lora_Bs),
    }
    nc = bacc.Bacc("TRN2", target_bir_lowering=False, num_devices=1)
    args = [nc.dram_tensor(name, a.shape, mybir.dt.from_np(a.dtype), kind="ExternalInput").ap()
            for name, a in arrays.items()]
    yT = nc.dram_tensor("yT", (nb, nt, P, tok), F32, kind="ExternalOutput").ap()
    build(nc, *args, yT)
    r = run_bass_kernel_spmd(nc, [arrays], core_ids=[0])
    return c(r.results[0]["yT"].reshape(nb, d, tok).transpose(0, 2, 1))
```

```python
from contextlib import ExitStack

import concourse.bass as bass
from concourse import mybir

P = 128
F32 = mybir.dt.float32
F32R = mybir.dt.float32r
I32 = mybir.dt.int32
ALU = mybir.AluOpType
ACT = mybir.ActivationFunctionType

LORA_SCALING = 32.0 / 16.0


def build(nc, xT, ids0, ids1, w0T, w1T, bias, lora_a, lora_b, yT):
    NB, XCHUNKS, _, KX, TOK = xT.shape
    ADAPTERS, NT, _, KT, _ = w0T.shape
    SLOTS, _, _, R = lora_a.shape
    D = KT * P
    RAW = 2
    PARTS = 2
    KP = KT // PARTS
    TILES = 2 * NT
    GROUP = 2 * R
    FIRST_W = [0, XCHUNKS // 2]
    XSYNC = 2
    assert GROUP == 32 and NT % 2 == 0 and XCHUNKS == NT // 2 and KX * XCHUNKS == KT

    with ExitStack() as ctx:
        def sb(name, shape, dt=F32):
            return ctx.enter_context(nc.sbuf_tensor(name, shape, dt))

        def psum(name, shape):
            return ctx.enter_context(nc.psum_tensor(name, shape, F32))

        def sem(name):
            return ctx.enter_context(nc.semaphore(name))

        x_hi = sb("x_hi", [P, KT, TOK], F32R)
        x_lo = sb("x_lo", [P, KT, TOK], F32R)
        x1_hi = sb("x1_hi", [P, KT, TOK], F32R)
        x1_lo = sb("x1_lo", [P, KT, TOK], F32R)
        w_raw = [sb(f"w_raw{s}", [P, KT, P]) for s in range(RAW)]
        w_hi = [sb(f"w_hi{s}", [P, KT, P], F32R) for s in range(RAW)]
        w_lo = [sb(f"w_lo{s}", [P, KT, P], F32R) for s in range(RAW)]
        a_raw = sb("a_raw", [P, KT, R])
        a_mix = sb("a_mix", [P, KT, P // GROUP, GROUP], F32R)
        b_raw = sb("b_raw", [P, D])
        b_mix = [sb(f"b_mix{s}", [P, P], F32R) for s in range(RAW)]
        h_mix = sb("h_mix", [P, TOK], F32R)
        bias_sb = sb("bias_sb", [P, NT])
        ids_sb = sb("ids_sb", [1, 2, NB], I32)
        out_slots = sb("out_slots", [P, RAW, TOK])
        x1_raw = y_out = out_slots[:]
        x_raw = sb("x_raw", [P, KX, TOK])[:]
        b_halves = b_raw[:].rearrange("p (h k n) -> p h k n", h=2, k=KX)
        x_first = [x_raw, out_slots[:], b_halves[:, 0], b_halves[:, 1]]

        sums = [psum(f"sums{s}", [P, TOK]) for s in range(RAW)]
        h_sum = psum("h_sum", [P, TOK])

        ids_loaded = sem("ids_loaded")
        bias_loaded = sem("bias_loaded")
        w_loaded = [[sem(f"w_loaded{s}_{part}") for part in range(PARTS)] for s in range(RAW)]
        w_raw_free = sem("w_raw_free")
        w_hi_done = sem("w_hi_done")
        w_ready = sem("w_ready")
        x_loaded = sem("x_loaded")
        x_first_loaded = [sem(f"x_first_loaded{i}") for i in range(XCHUNKS)]
        x_hi_done = sem("x_hi_done")
        x_ready = sem("x_ready")
        a_loaded = sem("a_loaded")
        b_loaded = sem("b_loaded")
        a_hi_done = sem("a_hi_done")
        a_ready = sem("a_ready")
        b_hi_done = sem("b_hi_done")
        b_ready = sem("b_ready")
        tile_done = sem("tile_done")
        sums_free = sem("sums_free")
        x1_part = sem("x1_part")
        x1_sum = sem("x1_sum")
        x1_hi_done = sem("x1_hi_done")
        x1_ready = sem("x1_ready")
        h_done = sem("h_done")
        h_hi_done = sem("h_hi_done")
        h_ready = sem("h_ready")
        y_part = sem("y_part")
        y_ready = sem("y_ready")
        y_stored = sem("y_stored")
        y_slot_free = sem("y_slot_free")

        block = ctx.enter_context(nc.Block())

        @block.sync
        def _(sp):
            sp.dma_start(ids_sb[:, 0, :], ids0).then_inc(ids_loaded, 16)
            sp.dma_start(ids_sb[:, 1, :], ids1).then_inc(ids_loaded, 16)
            for chunk in range(XSYNC):
                sp.dma_start(x_first[chunk], xT[0, chunk]).then_inc(x_first_loaded[chunk], 16)
            sp.dma_start(bias_sb[:], bias).then_inc(bias_loaded, 16)
            sp.wait_ge(ids_loaded, 32)
            with sp.Fori(0, NB) as b:
                adapter = sp.value_load(ids_sb[0:1, 0, bass.ds(b, 1)], min_val=0, max_val=ADAPTERS - 1)
                with sp.Fori(0, NT // 2) as pair:
                    for s in range(RAW):
                        sp.wait_ge(w_raw_free, b * TILES + pair * 2 + s + 1)
                        for part in range(PARTS):
                            ks = slice(part * KP, (part + 1) * KP)
                            sp.dma_start(w_raw[s][:, ks], w0T[bass.ds(adapter, 1), bass.ds(pair * 2 + s, 1), :, ks]
                                         .rearrange("a t p k o -> (a t p) k o")).then_inc(w_loaded[s][part], 16)
                with sp.Fori(0, NT // 2) as pair:
                    for s in range(RAW):
                        sp.wait_ge(w_raw_free, b * TILES + NT + pair * 2 + s + 1)
                        for part in range(PARTS):
                            ks = slice(part * KP, (part + 1) * KP)
                            sp.dma_start(w_raw[s][:, ks], w1T[bass.ds(pair * 2 + s, 1), :, ks]
                                         .rearrange("t p k o -> (t p) k o")).then_inc(w_loaded[s][part], 16)

        @block.gpsimd
        def _(pool):
            pool.sem_inc(y_slot_free, RAW)

            def load_x(b, chunk):
                pool.dma_start(x_raw, xT[bass.ds(b, 1), bass.ds(chunk, 1)]
                               .rearrange("b c p k n -> (b c p) k n")).then_inc(x_loaded, 16)

            def load_a(b):
                slot = pool.value_load(ids_sb[0:1, 1, bass.ds(b, 1)], min_val=0, max_val=SLOTS - 1)
                pool.dma_start(a_raw[:], lora_a[bass.ds(slot, 1)]
                               .rearrange("s p k r -> (s p) k r")).then_inc(a_loaded, 16)

            pool.wait_ge(ids_loaded, 32)
            for chunk in range(XSYNC, XCHUNKS):
                if chunk >= len(x_first):
                    pool.wait_ge(x_ready, chunk - len(x_first) + 1)
                pool.dma_start(x_first[chunk % len(x_first)], xT[0, chunk]).then_inc(x_first_loaded[chunk], 16)
            load_a(0)
            with pool.Fori(0, NB) as b:
                slot = pool.value_load(ids_sb[0:1, 1, bass.ds(b, 1)], min_val=0, max_val=SLOTS - 1)
                pool.wait_ge(x_ready, (b + 1) * XCHUNKS)
                for copy in range(P // R):
                    pool.dma_start(b_raw[copy * R:(copy + 1) * R, :], lora_b[bass.ds(slot, 1)]
                                   .rearrange("s r n -> (s r) n")).then_inc(b_loaded, 16)
                with pool.If(b < NB - 1):
                    pool.wait_ge(a_ready, (b + 1) * (P // GROUP))
                    load_a(nc.s_assert_within(
                        b + 1, 1, NB - 1, skip_runtime_bounds_check_because="only where b < NB - 1"))
                with pool.Fori(0, NT // 2) as pair:
                    with pool.If(b < NB - 1):
                        pool.wait_ge(x_ready, (b + 1) * XCHUNKS + pair)
                        load_x(nc.s_assert_within(
                            b + 1, 1, NB - 1, skip_runtime_bounds_check_because="only where b < NB - 1"), pair)
                    for s in range(RAW):
                        pool.wait_ge(y_ready, b * NT + pair * 2 + s + 1)
                        pool.dma_start(yT[bass.ds(b, 1), bass.ds(pair * 2 + s, 1)]
                                       .rearrange("b t p n -> (b t p) n"), y_out[:, s, :]
                                       ).then_inc(y_stored, 16)
                        pool.wait_ge(y_stored, (b * NT + pair * 2 + s + 1) * 16)
                        pool.sem_inc(y_slot_free, 1)

        @block.scalar
        def _(act):
            def w_hi_part(s, n, part):
                act.wait_ge(w_loaded[s][part], (n - s) * (16 // RAW) + 16)
                ks = slice(part * KP, (part + 1) * KP)
                act.activation(w_hi[s][:, ks], w_raw[s][:, ks], ACT.Copy).then_inc(w_hi_done, 1)

            def x_hi_part(b, chunk):
                act.wait_ge(x_loaded, ((b - 1) * XCHUNKS + chunk + 1) * 16)
                act.activation(x_hi[:, bass.ds(chunk * KX, KX), :], x_raw, ACT.Copy).then_inc(x_hi_done, 1)

            for chunk in range(XCHUNKS):
                if chunk in FIRST_W:
                    w_hi_part(0, 0, FIRST_W.index(chunk))
                act.wait_ge(x_first_loaded[chunk], 16)
                act.activation(x_hi[:, chunk * KX:(chunk + 1) * KX, :], x_first[chunk % len(x_first)],
                               ACT.Copy).then_inc(x_hi_done, 1)
            for part in range(PARTS):
                w_hi_part(1, 1, part)
            with act.Fori(0, NB) as b:
                act.wait_ge(a_loaded, (b + 1) * 16)
                for q in range(P // GROUP):
                    act.activation(a_mix[:, :, q, 0:R], a_raw[:], ACT.Copy).then_inc(a_hi_done, 1)
                with act.Fori(0, NT // 2) as pair:
                    for s in range(RAW):
                        n = b * TILES + pair * 2 + s
                        act.wait_ge(tile_done, n + 1)
                        for part in range(PARTS):
                            w_hi_part(s, n + RAW, part)
                        act.wait_ge(x1_sum, b * NT + pair * 2 + s + 1)
                        act.activation(x1_hi[:, bass.ds(pair * 2 + s, 1), :], x1_raw[:, s:s + 1, :],
                                       ACT.Copy).then_inc(x1_hi_done, 1)
                act.wait_ge(h_done, b + 1)
                act.activation(h_mix[:], h_sum[:], ACT.Copy).then_inc(h_hi_done, 1)
                act.wait_ge(b_loaded, (b + 1) * (16 * (P // R)))
                with act.Fori(0, NT // 2) as pair:
                    for s in range(RAW):
                        t = pair * 2 + s
                        n = b * TILES + NT + t
                        act.activation(b_mix[s][:], b_raw[:, bass.ds(t * P, P)], ACT.Copy,
                                       scale=LORA_SCALING).then_inc(b_hi_done, 1)
                        with act.If(n < NB * TILES - RAW):
                            act.wait_ge(tile_done, n + 1)
                            for part in range(PARTS):
                                w_hi_part(s, n + RAW, part)
                    with act.If(b < NB - 1):
                        act.wait_ge(x1_ready, (b + 1) * NT)
                        x_hi_part(b + 1, pair)

        @block.vector
        def _(dve):
            dve.sem_inc(w_raw_free, 1)
            dve.sem_inc(sums_free, RAW)

            def w_lo_part(s, n, part):
                count = n * PARTS + part + 1
                ks = slice(part * KP, (part + 1) * KP)
                dve.wait_ge(w_hi_done, count)
                dve.tensor_tensor(w_lo[s][:, ks], w_raw[s][:, ks], w_hi[s][:, ks].bitcast(F32),
                                  ALU.subtract).then_inc(w_ready, 1)
                if part == PARTS - 1:
                    dve.wait_ge(w_ready, count)
                    dve.sem_inc(w_raw_free, 1)

            def x_lo_part(b, chunk):
                dve.wait_ge(x_hi_done, b * XCHUNKS + chunk + 1)
                dve.tensor_tensor(x_lo[:, bass.ds(chunk * KX, KX), :], x_raw,
                                  x_hi[:, bass.ds(chunk * KX, KX), :].bitcast(F32),
                                  ALU.subtract).then_inc(x_ready, 1)

            for chunk in range(XCHUNKS):
                if chunk in FIRST_W:
                    w_lo_part(0, 0, FIRST_W.index(chunk))
                dve.wait_ge(x_hi_done, chunk + 1)
                dve.tensor_tensor(x_lo[:, chunk * KX:(chunk + 1) * KX, :], x_first[chunk % len(x_first)],
                                  x_hi[:, chunk * KX:(chunk + 1) * KX, :].bitcast(F32),
                                  ALU.subtract).then_inc(x_ready, 1)
                if chunk == len(x_first) - 1:
                    dve.sem_inc(w_raw_free, 1)
            for part in range(PARTS):
                w_lo_part(1, 1, part)
            dve.wait_ge(bias_loaded, 16)
            with dve.Fori(0, NB) as b:
                dve.wait_ge(y_slot_free, b * NT + RAW)
                dve.wait_ge(a_hi_done, (b + 1) * (P // GROUP))
                for q in range(P // GROUP):
                    dve.tensor_tensor(a_mix[:, :, q, R:GROUP], a_raw[:], a_mix[:, :, q, 0:R].bitcast(F32),
                                      ALU.subtract).then_inc(a_ready, 1)
                with dve.Fori(0, NT // 2) as pair:
                    for s in range(RAW):
                        t = pair * 2 + s
                        n = b * TILES + t
                        dve.wait_ge(tile_done, n + 1)
                        dve.tensor_tensor(x1_raw[:, s:s + 1, :], sums[s][:].unsqueeze(1),
                                          x_lo[:, bass.ds(t, 1), :].bitcast(F32),
                                          ALU.add).then_inc(x1_part, 1)
                        dve.wait_ge(x1_part, b * NT + t + 1)
                        dve.sem_inc(sums_free, 1)
                        dve.tensor_tensor(x1_raw[:, s:s + 1, :], x1_raw[:, s:s + 1, :],
                                          x_hi[:, bass.ds(t, 1), :].bitcast(F32),
                                          ALU.add).then_inc(x1_sum, 1)
                        dve.wait_ge(x1_hi_done, b * NT + t + 1)
                        dve.tensor_tensor(x1_lo[:, bass.ds(t, 1), :], x1_raw[:, s:s + 1, :],
                                          x1_hi[:, bass.ds(t, 1), :].bitcast(F32),
                                          ALU.subtract).then_inc(x1_ready, 1)
                        for part in range(PARTS):
                            w_lo_part(s, n + RAW, part)
                dve.wait_ge(h_hi_done, b + 1)
                for q in range(1, P // GROUP, 2):
                    rows = slice(q * GROUP, (q + 1) * GROUP)
                    dve.tensor_tensor(h_mix[rows, :], h_sum[rows, :], h_mix[rows, :].bitcast(F32),
                                      ALU.subtract).then_inc(h_ready, 1)
                with dve.Fori(0, NT // 2) as pair:
                    for s in range(RAW):
                        t = pair * 2 + s
                        n = b * TILES + NT + t
                        dve.wait_ge(b_hi_done, b * NT + t + 1)
                        dve.scalar_tensor_tensor(out=b_mix[s][P // 2:P, :],
                                                 in0=b_raw[P // 2:P, bass.ds(t * P, P)], scalar=LORA_SCALING,
                                                 in1=b_mix[s][P // 2:P, :].bitcast(F32), op0=ALU.mult,
                                                 op1=ALU.subtract).then_inc(b_ready, 1)
                        dve.wait_ge(tile_done, n + 1)
                        dve.wait_ge(y_slot_free, b * NT + t + 1)
                        dve.scalar_tensor_tensor(out=y_out[:, s, :], in0=sums[s][:],
                                                 scalar=bias_sb[:, bass.ds(t, 1)],
                                                 in1=x1_lo[:, bass.ds(t, 1), :].squeeze(1).bitcast(F32),
                                                 op0=ALU.add, op1=ALU.add).then_inc(y_part, 1)
                        dve.wait_ge(y_part, b * NT + t + 1)
                        dve.sem_inc(sums_free, 1)
                        dve.tensor_tensor(y_out[:, s:s + 1, :], y_out[:, s:s + 1, :],
                                          x1_hi[:, bass.ds(t, 1), :].bitcast(F32),
                                          ALU.add).then_inc(y_ready, 1)
                        with dve.If(n < NB * TILES - RAW):
                            for part in range(PARTS):
                                w_lo_part(s, n + RAW, part)
                    with dve.If(b < NB - 1):
                        x_lo_part(b + 1, pair)

        @block.tensor
        def _(pe):
            def tile(s, n, hi, lo, wait_k, last):
                pe.wait_ge(sums_free, n + 1)
                for k in range(KT):
                    if k % KP == 0:
                        pe.wait_ge(w_ready, n * PARTS + k // KP + 1)
                    wait_k(k)
                    pe.matmul(sums[s][:], w_hi[s][:, k, :], hi[:, k, :], start=(k == 0), stop=False)
                    pe.matmul(sums[s][:], w_hi[s][:, k, :], lo[:, k, :], start=False, stop=False)
                    mm = pe.matmul(sums[s][:], w_lo[s][:, k, :], hi[:, k, :], start=False,
                                   stop=last and k == KT - 1)
                return mm

            with pe.Fori(0, NB) as b:
                with pe.Fori(0, NT // 2) as pair:
                    for s in range(RAW):
                        def x_chunk_ready(k, s=s):
                            if s == 0 and k % KX == 0:
                                pe.wait_ge(x_ready, b * XCHUNKS + k // KX + 1)
                        tile(s, b * TILES + pair * 2 + s, x_hi, x_lo, x_chunk_ready, True).then_inc(tile_done, 1)
                pe.wait_ge(a_ready, (b + 1) * (P // GROUP))
                pe.wait_ge(x1_ready, b * NT + NT - 1)
                for k in range(KT):
                    if k == KT - 1:
                        pe.wait_ge(x1_ready, b * NT + NT)
                    a_k = a_mix[:, k, :, :].rearrange("p q r -> p (q r)")
                    pe.matmul(h_sum[:], a_k, x1_hi[:, k, :], start=(k == 0), stop=False)
                    mm = pe.matmul(h_sum[:], a_k, x1_lo[:, k, :], start=False, stop=(k == KT - 1))
                mm.then_inc(h_done, 1)
                with pe.Fori(0, NT // 2) as pair:
                    for s in range(RAW):
                        t = pair * 2 + s
                        tile(s, b * TILES + NT + t, x1_hi, x1_lo, lambda k: None, False)
                        pe.wait_ge(h_ready, (b + 1) * 2)
                        pe.wait_ge(b_ready, b * NT + t + 1)
                        pe.matmul(sums[s][:], b_mix[s][:], h_mix[:], start=False,
                                  stop=True).then_inc(tile_done, 1)


def kernel(x, itok_B_3_7, itok_B_0_23, L0_cond_weight, L1_cond_W, L1_cond_b, L1_cond_lora_As, L1_cond_lora_Bs):
    import numpy as np
    import concourse.bacc as bacc
    from concourse.bass_utils import run_bass_kernel_spmd

    nb, tok, d = x.shape
    nt, kt, kx = d // P, d // P, 2
    c = np.ascontiguousarray
    arrays = {
        "xT": c(x.reshape(nb, tok, kt // kx, kx, P).transpose(0, 2, 4, 3, 1)),
        "ids0": c(itok_B_3_7.reshape(1, nb)),
        "ids1": c(itok_B_0_23.reshape(1, nb)),
        "w0T": c(L0_cond_weight.reshape(-1, nt, P, kt, P).transpose(0, 1, 4, 3, 2)),
        "w1T": c(L1_cond_W.reshape(nt, P, kt, P).transpose(0, 3, 2, 1)),
        "bias": c(L1_cond_b.reshape(nt, P).T),
        "lora_a": c(L1_cond_lora_As.reshape(-1, kt, P, L1_cond_lora_As.shape[2]).transpose(0, 2, 1, 3)),
        "lora_b": c(L1_cond_lora_Bs),
    }
    nc = bacc.Bacc("TRN2", target_bir_lowering=False, num_devices=1)
    args = [nc.dram_tensor(name, a.shape, mybir.dt.from_np(a.dtype), kind="ExternalInput").ap()
            for name, a in arrays.items()]
    yT = nc.dram_tensor("yT", (nb, nt, P, tok), F32, kind="ExternalOutput").ap()
    build(nc, *args, yT)
    r = run_bass_kernel_spmd(nc, [arrays], core_ids=[0])
    return c(r.results[0]["yT"].reshape(nb, d, tok).transpose(0, 2, 1))
```
